# Optimizing a Trainium2 kernel written in Bass

```python
import numpy as np
import jax
import jax.numpy as jnp

def _softmax(x, axis=-1):
    return jax.nn.softmax(x, axis=axis)

def _gelu(x):
    return jax.nn.gelu(x, approximate=True)

def _silu(x):
    return jax.nn.silu(x)

def _sigmoid(x):
    return jax.nn.sigmoid(x)

def _layernorm(x, axis=-1, eps=1e-05):
    m = jnp.mean(x, axis=axis, keepdims=True)
    v = jnp.var(x, axis=axis, keepdims=True)
    return (x - m) / jnp.sqrt(v + eps)

def _scatter_add(tgt, idx, src, axis=0):
    return tgt.at[idx].add(src)

def _segment_sum(src, seg, n):
    return jax.ops.segment_sum(src, seg, n)
kernel_name = 'mk_dlrm_tower_d1_rec_r8_1706a5'

def setup_inputs(seed: int=0):
    np.random.seed(seed)
    _w = jnp.asarray

    def _rec_inputs():
        import jax
        import jax.numpy as jnp
        _tk = jax.random.key(seed)
        ids = jnp.stack([jax.random.randint(jax.random.fold_in(_tk, 200 + f), (512,), 0, v, jnp.int32) for f, v in enumerate([12500, 1000, 12500, 125000, 12500, 12500, 1250, 12500, 1000, 12500, 12500, 12500, 1250, 1250, 1000, 12500, 1250, 1000, 1000, 1000, 1000, 1000, 1000, 1000, 1000, 1000])], axis=1)
        tbl_0 = 0.05 * jax.random.normal(jax.random.fold_in(_tk, 500 + 0), (12500, 128), jnp.float32)
        tbl_1 = 0.05 * jax.random.normal(jax.random.fold_in(_tk, 500 + 1), (1000, 128), jnp.float32)
        tbl_2 = 0.05 * jax.random.normal(jax.random.fold_in(_tk, 500 + 2), (12500, 128), jnp.float32)
        tbl_3 = 0.05 * jax.random.normal(jax.random.fold_in(_tk, 500 + 3), (125000, 128), jnp.float32)
        tbl_4 = 0.05 * jax.random.normal(jax.random.fold_in(_tk, 500 + 4), (12500, 128), jnp.float32)
        tbl_5 = 0.05 * jax.random.normal(jax.random.fold_in(_tk, 500 + 5), (12500, 128), jnp.float32)
        tbl_6 = 0.05 * jax.random.normal(jax.random.fold_in(_tk, 500 + 6), (1250, 128), jnp.float32)
        tbl_7 = 0.05 * jax.random.normal(jax.random.fold_in(_tk, 500 + 7), (12500, 128), jnp.float32)
        tbl_8 = 0.05 * jax.random.normal(jax.random.fold_in(_tk, 500 + 8), (1000, 128), jnp.float32)
        tbl_9 = 0.05 * jax.random.normal(jax.random.fold_in(_tk, 500 + 9), (12500, 128), jnp.float32)
        tbl_10 = 0.05 * jax.random.normal(jax.random.fold_in(_tk, 500 + 10), (12500, 128), jnp.float32)
        tbl_11 = 0.05 * jax.random.normal(jax.random.fold_in(_tk, 500 + 11), (12500, 128), jnp.float32)
        tbl_12 = 0.05 * jax.random.normal(jax.random.fold_in(_tk, 500 + 12), (1250, 128), jnp.float32)
        tbl_13 = 0.05 * jax.random.normal(jax.random.fold_in(_tk, 500 + 13), (1250, 128), jnp.float32)
        tbl_14 = 0.05 * jax.random.normal(jax.random.fold_in(_tk, 500 + 14), (1000, 128), jnp.float32)
        tbl_15 = 0.05 * jax.random.normal(jax.random.fold_in(_tk, 500 + 15), (12500, 128), jnp.float32)
        tbl_16 = 0.05 * jax.random.normal(jax.random.fold_in(_tk, 500 + 16), (1250, 128), jnp.float32)
        tbl_17 = 0.05 * jax.random.normal(jax.random.fold_in(_tk, 500 + 17), (1000, 128), jnp.float32)
        tbl_18 = 0.05 * jax.random.normal(jax.random.fold_in(_tk, 500 + 18), (1000, 128), jnp.float32)
        tbl_19 = 0.05 * jax.random.normal(jax.random.fold_in(_tk, 500 + 19), (1000, 128), jnp.float32)
        tbl_20 = 0.05 * jax.random.normal(jax.random.fold_in(_tk, 500 + 20), (1000, 128), jnp.float32)
        tbl_21 = 0.05 * jax.random.normal(jax.random.fold_in(_tk, 500 + 21), (1000, 128), jnp.float32)
        tbl_22 = 0.05 * jax.random.normal(jax.random.fold_in(_tk, 500 + 22), (1000, 128), jnp.float32)
        tbl_23 = 0.05 * jax.random.normal(jax.random.fold_in(_tk, 500 + 23), (1000, 128), jnp.float32)
        tbl_24 = 0.05 * jax.random.normal(jax.random.fold_in(_tk, 500 + 24), (1000, 128), jnp.float32)
        tbl_25 = 0.05 * jax.random.normal(jax.random.fold_in(_tk, 500 + 25), (1000, 128), jnp.float32)
        _rk = jax.random.fold_in(_tk, 7)
        r_dense_features = 7.22013e-05 + 1.00017 * jax.random.normal(jax.random.fold_in(_rk, 101), (512, 128), jnp.float32)
        W_top1 = 0.0456912 * jax.random.normal(jax.random.fold_in(_tk, 801), (479, 512), jnp.float32)
        W_top2 = 0.0441942 * jax.random.normal(jax.random.fold_in(_tk, 802), (512, 256), jnp.float32)
        W_top3 = 0.0625 * jax.random.normal(jax.random.fold_in(_tk, 803), (256, 1), jnp.float32)
        b_top1 = jnp.zeros((512,), jnp.float32)
        b_top2 = jnp.zeros((256,), jnp.float32)
        return (r_dense_features, ids, tbl_0, tbl_1, tbl_2, tbl_3, tbl_4, tbl_5, tbl_6, tbl_7, tbl_8, tbl_9, tbl_10, tbl_11, tbl_12, tbl_13, tbl_14, tbl_15, tbl_16, tbl_17, tbl_18, tbl_19, tbl_20, tbl_21, tbl_22, tbl_23, tbl_24, tbl_25, W_top1, b_top1, W_top2, b_top2, W_top3)
    r_dense_features, ids, tbl_0, tbl_1, tbl_2, tbl_3, tbl_4, tbl_5, tbl_6, tbl_7, tbl_8, tbl_9, tbl_10, tbl_11, tbl_12, tbl_13, tbl_14, tbl_15, tbl_16, tbl_17, tbl_18, tbl_19, tbl_20, tbl_21, tbl_22, tbl_23, tbl_24, tbl_25, W_top1, b_top1, W_top2, b_top2, W_top3 = _rec_inputs()

    def _L0_rec_setup():
        import jax, jax.numpy as jnp
        import numpy as np
        FEATURE_NUM = 27
        key = jax.random.key(seed)
        k1, k2 = jax.random.split(key)
        B, N, D = (8192, FEATURE_NUM - 1, 128)
        dense_features = jax.random.normal(k1, (B, D), dtype=jnp.float32)
        sparse_features = jax.random.normal(k2, (B, N, D), dtype=jnp.float32)
        return {'dense_features': dense_features, 'sparse_features': sparse_features}
    _L0_rec_all = _L0_rec_setup()
    _L0_rec_in = {k: v for k, v in _L0_rec_all.items() if k in ()}
    del _L0_rec_all
    return {'r_dense_features': r_dense_features, 'ids': ids, 'tbl_0': tbl_0, 'tbl_1': tbl_1, 'tbl_2': tbl_2, 'tbl_3': tbl_3, 'tbl_4': tbl_4, 'tbl_5': tbl_5, 'tbl_6': tbl_6, 'tbl_7': tbl_7, 'tbl_8': tbl_8, 'tbl_9': tbl_9, 'tbl_10': tbl_10, 'tbl_11': tbl_11, 'tbl_12': tbl_12, 'tbl_13': tbl_13, 'tbl_14': tbl_14, 'tbl_15': tbl_15, 'tbl_16': tbl_16, 'tbl_17': tbl_17, 'tbl_18': tbl_18, 'tbl_19': tbl_19, 'tbl_20': tbl_20, 'tbl_21': tbl_21, 'tbl_22': tbl_22, 'tbl_23': tbl_23, 'tbl_24': tbl_24, 'tbl_25': tbl_25, 'W_top1': W_top1, 'b_top1': b_top1, 'W_top2': W_top2, 'b_top2': b_top2, 'W_top3': W_top3}

def reference(r_dense_features, ids, tbl_0, tbl_1, tbl_2, tbl_3, tbl_4, tbl_5, tbl_6, tbl_7, tbl_8, tbl_9, tbl_10, tbl_11, tbl_12, tbl_13, tbl_14, tbl_15, tbl_16, tbl_17, tbl_18, tbl_19, tbl_20, tbl_21, tbl_22, tbl_23, tbl_24, tbl_25, W_top1, b_top1, W_top2, b_top2, W_top3):
    import jax
    import jax.numpy as jnp

    def _L0_rec_ref(dense_features, sparse_features):
        import jax, jax.numpy as jnp
        import numpy as np
        FEATURE_NUM = 27
        combined = jnp.concatenate([dense_features[:, None, :], sparse_features], axis=1)
        interactions = jnp.einsum('bfd,bgd->bfg', combined, combined)
        iu, ju = jnp.triu_indices(FEATURE_NUM, k=1)
        return interactions[:, iu, ju]
    e = jnp.stack([tbl_0[ids[:, 0]], tbl_1[ids[:, 1]], tbl_2[ids[:, 2]], tbl_3[ids[:, 3]], tbl_4[ids[:, 4]], tbl_5[ids[:, 5]], tbl_6[ids[:, 6]], tbl_7[ids[:, 7]], tbl_8[ids[:, 8]], tbl_9[ids[:, 9]], tbl_10[ids[:, 10]], tbl_11[ids[:, 11]], tbl_12[ids[:, 12]], tbl_13[ids[:, 13]], tbl_14[ids[:, 14]], tbl_15[ids[:, 15]], tbl_16[ids[:, 16]], tbl_17[ids[:, 17]], tbl_18[ids[:, 18]], tbl_19[ids[:, 19]], tbl_20[ids[:, 20]], tbl_21[ids[:, 21]], tbl_22[ids[:, 22]], tbl_23[ids[:, 23]], tbl_24[ids[:, 24]], tbl_25[ids[:, 25]]], axis=1)
    z = _L0_rec_ref(r_dense_features, e)
    z = z.reshape(z.shape[0], -1)
    h = jnp.concatenate([z, r_dense_features], axis=1)
    h = jnp.maximum(h @ W_top1 + b_top1, 0.0)
    h = jnp.maximum(h @ W_top2 + b_top2, 0.0)
    y = h @ W_top3
    return y

_drawn_inputs = setup_inputs


def setup_inputs(seed=0):
    import zlib

    import numpy as np

    out = dict(_drawn_inputs(seed))
    spreads = {'b_top1': (0.0, 0.1), 'b_top2': (0.0, 0.1)}
    factors = {}
    for name, (base, spread) in spreads.items():
        noise = np.random.default_rng([zlib.crc32(name.encode()), seed]).standard_normal(out[name].shape)
        drawn = base * np.exp(spread * noise) if base else spread * noise
        out[name] = jnp.asarray(drawn.astype(out[name].dtype))
    for name, factor in factors.items():
        out[name] = (out[name] * factor).astype(out[name].dtype)
    return out
```

```python
import concourse.bass as bass
import concourse.mybir as mybir
import numpy as np
from contextlib import ExitStack

P = 128
BATCH = 512
DIM = 128
TABLES = 26
FEATURES = TABLES + 1
HIDDEN1, HIDDEN2 = 512, 256

TILES = BATCH // P
QUAD = 4
LANE = P // QUAD
COLS = 28
SLOTS = COLS // QUAD
CHUNKS1 = HIDDEN1 // P
CHUNKS2 = HIDDEN2 // P

GROUP = 4
GROUPS = [list(range(a, min(a + GROUP, TABLES))) for a in range(0, TABLES, GROUP)]
EVEN = len(GROUPS[0::2])
ODD = len(GROUPS[1::2])

PER_BANK = 4
PER_ROUND = 2 * PER_BANK
ROUNDS = P // QUAD // PER_ROUND


def dlrm_tower(nc, dense_t, ids, tables, w1, w2, w3, b1, b2, out):
    fp32, u32 = mybir.dt.float32, mybir.dt.uint32
    ALU, ACT = mybir.AluOpType, mybir.ActivationFunctionType

    ctx = ExitStack()
    with ctx:
        def sb(name, shape, dt=fp32):
            return ctx.enter_context(nc.sbuf_tensor(name, shape, dt))

        def ps(name, shape):
            return ctx.enter_context(nc.psum_tensor(name, shape, fp32))

        def sem(name):
            return ctx.enter_context(nc.semaphore(name))

        ident = sb("ident", [P, P])
        index = sb("index", [P, TILES, TABLES], u32)
        rows = sb("rows", [P, TABLES, DIM])
        dense_sb = sb("dense_sb", [P, BATCH])
        turned = sb("turned", [P, P, LANE])
        pairs = sb("pairs", [P, SLOTS, P])
        w1_sb = sb("w1_sb", [P, SLOTS + 1, HIDDEN1])
        w2_sb = sb("w2_sb", [P, CHUNKS1, HIDDEN2])
        w3_sb = sb("w3_sb", [P, CHUNKS2])
        b1_sb = sb("b1_sb", [P, CHUNKS1])
        b2_sb = sb("b2_sb", [P, CHUNKS2])
        hid1 = sb("hid1", [P, CHUNKS1, P])
        hid2 = sb("hid2", [P, CHUNKS2, P])
        y_sb = sb("y_sb", [1, BATCH])

        turn_ps = [ps(f"turn_ps{n}", [P, GROUP, P]) for n in range(2)]
        gram_ps = [ps(f"gram_ps{n}", [P, 2, PER_BANK, P]) for n in range(2)]
        hid1_ps = ps("hid1_ps", [P, CHUNKS1, P])
        hid2_ps = ps("hid2_ps", [P, CHUNKS2 + 1, P])

        ident_set = sem("ident_set")
        pad_set = sem("pad_set")
        index_in = sem("index_in")
        dense_in = sem("dense_in")
        w1_in = sem("w1_in")
        w2_in = sem("w2_in")
        small_in = sem("small_in")
        gathered = [sem(f"gathered{g}") for g in range(len(GROUPS))]
        turned_rows = sem("turned_rows")
        out_even = sem("out_even")
        out_odd = sem("out_odd")
        dense_placed = sem("dense_placed")
        gram_done = sem("gram_done")
        gram_free_v = sem("gram_free_v")
        gram_free_s = sem("gram_free_s")
        hid1_done = sem("hid1_done")
        hid1_out = sem("hid1_out")
        hid2_done = sem("hid2_done")
        hid2_out = sem("hid2_out")
        y_done = sem("y_done")
        y_out = sem("y_out")
        stored = sem("stored")

        block = ctx.enter_context(nc.Block())

        @block.sync
        def _(sp):
            sp.dma_start(index[:, :, :], ids).then_inc(index_in, 16)
            sp.dma_start(dense_sb[:, :], dense_t).then_inc(dense_in, 16)
            sp.dma_start(w1_sb[:, :, :], w1).then_inc(w1_in, 16)
            sp.dma_start(w2_sb[:, :, :], w2).then_inc(w2_in, 16)
            sp.dma_start(w3_sb[:, :], w3).then_inc(small_in, 16)
            sp.dma_start(b1_sb[:, :], b1).then_inc(small_in, 16)
            sp.dma_start(b2_sb[:, :], b2).then_inc(small_in, 16)
            sp.wait_ge(y_out, TILES + 1)
            sp.dma_start(out, y_sb[:, :]).then_inc(stored, 16)
            sp.wait_ge(stored, 16)

        @block.gpsimd
        def _(pool):
            nc.gpsimd.memset(ident[:, :], 0.0).then_inc(ident_set, 1)
            pool.wait_ge(ident_set, 1)
            nc.gpsimd.affine_select(out=ident[:, :], in_=ident[:, :], compare_op=ALU.not_equal, fill=1.0,
                                    base=0, pattern=[[-1, P]], channel_multiplier=1).then_inc(ident_set, 1)
            pool.wait_ge(index_in, 16)
            for t in range(TILES):
                for g, group in enumerate(GROUPS):
                    pool.wait_ge(turned_rows, t * len(GROUPS) + g + 1)
                    for f in group:
                        pool.indirect_dma_start(
                            rows[:, f, :], None, tables[f],
                            bass.IndirectOffsetOnAxis(ap=index[:, t, f:f + 1], axis=0),
                        ).then_inc(gathered[g], 16)

        @block.tensor
        def _(pe):
            pe.sem_inc(turned_rows, len(GROUPS))
            pe.sem_inc(gram_done, 1)
            pe.wait_ge(ident_set, 2)
            pe.wait_ge(w1_in, 16)
            pe.wait_ge(w2_in, 16)
            pe.wait_ge(small_in, 48)
            with pe.Fori(0, TILES) as t:
                for g, group in enumerate(GROUPS):
                    pe.wait_ge(gathered[g], t * (16 * len(group)) + 16 * len(group))
                    if g % 2 == 0:
                        pe.wait_ge(out_even, t * EVEN + (g // 2 + 1))
                    else:
                        pe.wait_ge(out_odd, t * ODD + (g // 2 + 1))
                    for n, f in enumerate(group):
                        last = nc.tensor.transpose(turn_ps[g % 2][:, n, :], rows[:, f, :], ident[:, :])
                    last.then_inc(turned_rows, 1)
                pe.wait_ge(out_even, t * EVEN + (EVEN + 1))
                pe.wait_ge(out_odd, t * ODD + (ODD + 1))
                pe.wait_ge(dense_placed, t + 1)
                for r in range(ROUNDS):
                    pe.wait_ge(gram_free_v, t * ROUNDS + r + 1)
                    pe.wait_ge(gram_free_s, t * ROUNDS + r + 1)
                    for n in range(PER_ROUND):
                        b = QUAD * (r * PER_ROUND + n)
                        last = nc.tensor.matmul(gram_ps[r % 2][:, n // PER_BANK, n % PER_BANK, 0:QUAD * COLS],
                                                turned[:, b:b + QUAD, :], turned[:, b:b + QUAD, 0:COLS],
                                                start=True, stop=True)
                    last.then_inc(gram_done, 1)
                pe.wait_ge(gram_free_v, t * ROUNDS + ROUNDS + 2)
                pe.wait_ge(gram_free_s, t * ROUNDS + ROUNDS + 2)
                pe.wait_ge(hid1_out, t + 1)
                for c in range(CHUNKS1):
                    for s in range(SLOTS + 1):
                        moving = pairs[:, s, :] if s < SLOTS else dense_sb[:, bass.ts(t, P)]
                        last = nc.tensor.matmul(hid1_ps[:, c, :], w1_sb[:, s, c * P:(c + 1) * P], moving,
                                                start=(s == 0), stop=(s == SLOTS))
                last.then_inc(hid1_done, 1)
                pe.wait_ge(hid1_out, t + 2)
                pe.wait_ge(y_out, t + 1)
                for c in range(CHUNKS2):
                    for k in range(CHUNKS1):
                        last = nc.tensor.matmul(hid2_ps[:, c, :], w2_sb[:, k, c * P:(c + 1) * P], hid1[:, k, :],
                                                start=(k == 0), stop=(k == CHUNKS1 - 1))
                last.then_inc(hid2_done, 1)
                pe.wait_ge(hid2_out, t + 1)
                for k in range(CHUNKS2):
                    last = nc.tensor.matmul(hid2_ps[0:1, CHUNKS2, :], w3_sb[:, k:k + 1], hid2[:, k, :],
                                            start=(k == 0), stop=(k == CHUNKS2 - 1))
                last.then_inc(y_done, 1)

        def bring_out_pairs(copy, r, quadrants):
            for q in quadrants:
                blocks = gram_ps[r % 2][LANE * q:LANE * (q + 1), :, :, q * COLS:(q + 1) * COLS]
                for g in range(QUAD):
                    to = pairs[LANE * g:LANE * (g + 1), :, r * PER_ROUND * QUAD:(r + 1) * PER_ROUND * QUAD]
                    last = copy(
                        to.rearrange("p s (k n q) -> p k n s q", k=2, q=QUAD)[:, :, :, :, q],
                        blocks.rearrange("p k n (s g) -> p k n s g", g=QUAD)[:, :, :, :, g])
            return last

        def bring_out_turned(copy, g):
            group = GROUPS[g]
            return copy(turned[:, :, 1 + group[0]:2 + group[-1]].rearrange("p b f -> p f b"),
                        turn_ps[g % 2][:, 0:len(group), :])

        @block.vector
        def _(dve):
            nc.vector.memset(turned[:, :, FEATURES:LANE], 0.0).then_inc(pad_set, 1)
            dve.wait_ge(pad_set, 1)
            dve.sem_inc(out_even, 1)
            dve.sem_inc(gram_free_v, 2)
            dve.wait_ge(dense_in, 16)
            with dve.Fori(0, TILES) as t:
                dve.wait_ge(gram_done, t * ROUNDS + 1)
                nc.vector.tensor_copy(turned[:, :, 0], dense_sb[:, bass.ts(t, P)]).then_inc(dense_placed, 1)
                for g in range(0, len(GROUPS), 2):
                    dve.wait_ge(turned_rows, t * len(GROUPS) + (len(GROUPS) + g + 1))
                    bring_out_turned(nc.vector.tensor_copy, g).then_inc(out_even, 1)
                for r in range(ROUNDS):
                    dve.wait_ge(gram_done, t * ROUNDS + (r + 2))
                    bring_out_pairs(nc.vector.tensor_copy, r, (0, 1)).then_inc(gram_free_v, 1)

        @block.scalar
        def _(act):
            act.sem_inc(out_odd, 1)
            act.sem_inc(gram_free_s, 2)
            act.sem_inc(hid1_out, 1)
            act.sem_inc(y_out, 1)
            act.wait_ge(small_in, 48)
            with act.Fori(0, TILES) as t:
                for g in range(1, len(GROUPS), 2):
                    act.wait_ge(turned_rows, t * len(GROUPS) + (len(GROUPS) + g + 1))
                    bring_out_turned(nc.scalar.copy, g).then_inc(out_odd, 1)
                for r in range(ROUNDS):
                    act.wait_ge(gram_done, t * ROUNDS + (r + 2))
                    bring_out_pairs(nc.scalar.copy, r, (2, 3)).then_inc(gram_free_s, 1)
                act.wait_ge(hid1_done, t + 1)
                for c in range(CHUNKS1):
                    last = nc.scalar.activation(hid1[:, c, :], hid1_ps[:, c, :], ACT.Relu, bias=b1_sb[:, c:c + 1])
                last.then_inc(hid1_out, 1)
                act.wait_ge(hid2_done, t + 1)
                for c in range(CHUNKS2):
                    last = nc.scalar.activation(hid2[:, c, :], hid2_ps[:, c, :], ACT.Relu, bias=b2_sb[:, c:c + 1])
                last.then_inc(hid2_out, 1)
                act.wait_ge(y_done, t + 1)
                nc.scalar.copy(y_sb[:, bass.ts(t, P)], hid2_ps[0:1, CHUNKS2, :]).then_inc(y_out, 1)


def lay_out_w1(w):
    laid = np.zeros((P, SLOTS + 1, HIDDEN1), w.dtype)
    pair = 0
    for i in range(FEATURES):
        for j in range(i + 1, FEATURES):
            laid[LANE * (j % QUAD) + i, j // QUAD] = w[pair]
            pair += 1
    laid[:, SLOTS] = w[pair:]
    return laid


def kernel(**inputs):
    import concourse.bacc as bacc
    from concourse.bass_utils import run_bass_kernel_spmd

    nc = bacc.Bacc("TRN2", target_bir_lowering=False, num_devices=1)
    arrays = {}

    def given(name, array):
        array = np.ascontiguousarray(array)
        arrays[name] = array
        return nc.dram_tensor(name, array.shape, mybir.dt.from_np(array.dtype), kind="ExternalInput").ap()

    x = {name: np.asarray(a) for name, a in inputs.items()}
    dense_t = given("dense_t", x["r_dense_features"].T)
    ids = given("ids", x["ids"].view(np.uint32).reshape(TILES, P, TABLES).transpose(1, 0, 2))
    tables = [given(f"tbl_{f}", x[f"tbl_{f}"]) for f in range(TABLES)]
    w1 = given("w1", lay_out_w1(x["W_top1"]))
    w2 = given("w2", x["W_top2"].reshape(CHUNKS1, P, HIDDEN2).transpose(1, 0, 2))
    w3 = given("w3", x["W_top3"].reshape(CHUNKS2, P).T)
    b1 = given("b1", x["b_top1"].reshape(CHUNKS1, P).T)
    b2 = given("b2", x["b_top2"].reshape(CHUNKS2, P).T)
    out = nc.dram_tensor("y", (1, BATCH), mybir.dt.float32, kind="ExternalOutput").ap()
    dlrm_tower(nc, dense_t, ids, tables, w1, w2, w3, b1, b2, out)
    result = run_bass_kernel_spmd(nc, [arrays], core_ids=[0])
    return result.results[0]["y"].reshape(BATCH, 1)
```

```python
import concourse.bass as bass
import concourse.mybir as mybir
import numpy as np
from contextlib import ExitStack

P = 128
BATCH = 512
DIM = 128
TABLES = 26
FEATURES = TABLES + 1
HIDDEN1, HIDDEN2 = 512, 256
TILES = BATCH // P
CHUNKS1 = HIDDEN1 // P
CHUNKS2 = HIDDEN2 // P

MATMUL_TABLES = [1, 8, 14, 17, 18, 19]
LOOKUPS = len(MATMUL_TABLES)
GATHER_TABLES = [f for f in range(TABLES) if f not in MATMUL_TABLES]
ROW_CHUNKS = 8
PADDED_ROWS = P * ROW_CHUNKS
ACT_CHUNKS = 1
DVE_CHUNKS = ROW_CHUNKS - ACT_CHUNKS
AHEAD = 3
PARTS = 2

RESIDENT = 1 + LOOKUPS
FEATURE_AT = [0] + [f + 1 for f in MATMUL_TABLES] + [f + 1 for f in GATHER_TABLES]

GROUP = 4
GROUPS = [list(range(a, min(a + GROUP, len(GATHER_TABLES)))) for a in range(0, len(GATHER_TABLES), GROUP)]
EVEN = len(GROUPS[0::2])
ODD = len(GROUPS[1::2])

FIRST_TURN = 2

QUAD = 4
LANE = P // QUAD
COLS = FEATURES - 1
SLOTS = -(-COLS // QUAD)
LAST_ROWS = LANE * (COLS - QUAD * (SLOTS - 1))
PER_BANK = 4
PER_ROUND = 2 * PER_BANK
ROUNDS = P // QUAD // PER_ROUND


def dlrm_tower(nc, dense_t, ids, ids_rows, tables, padded, w1, w2, w3, b1, b2, out):
    fp32, fp32r = mybir.dt.float32, mybir.dt.float32r
    i32, u32 = mybir.dt.int32, mybir.dt.uint32
    ALU, ACT = mybir.AluOpType, mybir.ActivationFunctionType

    ctx = ExitStack()
    with ctx:
        def sb(name, shape, dt=fp32):
            return ctx.enter_context(nc.sbuf_tensor(name, shape, dt))

        def ps(name, shape):
            return ctx.enter_context(nc.psum_tensor(name, shape, fp32))

        def sem(name):
            return ctx.enter_context(nc.semaphore(name))

        ident = sb("ident", [P, P])
        index = sb("index", [P, TILES, TABLES], u32)
        rows = sb("rows", [P, len(GATHER_TABLES), DIM])
        resident = sb("resident", [P, RESIDENT, BATCH])
        turned = sb("turned", [P, P, LANE])
        pairs = sb("pairs", [P, SLOTS, P])

        row_id_i = sb("row_id_i", [P, ROW_CHUNKS], i32)
        row_id = sb("row_id", [P, ROW_CHUNKS])
        minus_row_id = sb("minus_row_id", [P, ROW_CHUNKS])
        one = sb("one", [P, 1])
        distance = [sb(f"distance{n}", [P, ACT_CHUNKS, BATCH]) for n in range(2)]
        ids_i = sb("ids_i", [P, LOOKUPS, BATCH], i32)
        table_sb = sb("table_sb", [P, LOOKUPS, ROW_CHUNKS * DIM])
        parts = [sb(f"parts{n}", [P, PARTS, ROW_CHUNKS * DIM], fp32r) for n in range(2)]
        onehot = [sb(f"onehot{n}", [P, ROW_CHUNKS, BATCH], fp32r) for n in range(2)]

        w1_sb = sb("w1_sb", [P, SLOTS + 1, HIDDEN1])
        w2_sb = sb("w2_sb", [P, CHUNKS1, HIDDEN2])
        w3_sb = sb("w3_sb", [P, CHUNKS2])
        b1_sb = sb("b1_sb", [P, CHUNKS1])
        b2_sb = sb("b2_sb", [P, CHUNKS2])
        hid1 = sb("hid1", [P, CHUNKS1, P])
        hid2 = sb("hid2", [P, CHUNKS2, P])
        y_sb = sb("y_sb", [1, BATCH])

        turn_ps = [ps(f"turn_ps{n}", [P, GROUP, P]) for n in range(2)]
        gram_ps = [ps(f"gram_ps{n}", [P, 2, PER_BANK, P]) for n in range(2)]
        lookup_ps = [g[:, 0, :, :].rearrange("p n m -> p (n m)") for g in gram_ps]
        hid1_ps = ps("hid1_ps", [P, CHUNKS1, P])
        hid2_ps = ps("hid2_ps", [P, CHUNKS2, P])
        y_ps = hid1_ps[0:1, 0, :]

        ident_set = sem("ident_set")
        row_id_set = sem("row_id_set")
        row_id_cast = sem("row_id_cast")
        pad_set = sem("pad_set")
        index_in = sem("index_in")
        ids_in = [sem(f"ids_in{n}") for n in range(LOOKUPS)]
        table_in = [sem(f"table_in{n}") for n in range(LOOKUPS)]
        dense_in = sem("dense_in")
        w1_in = [sem(f"w1_in{s}") for s in range(SLOTS + 1)]
        w2_in = sem("w2_in")
        small_in = sem("small_in")
        high_set = sem("high_set")
        low_set = sem("low_set")
        onehot_set_v = sem("onehot_set_v")
        onehot_set_s = sem("onehot_set_s")
        distance_set = sem("distance_set")
        lookup_done = sem("lookup_done")
        lookup_out = sem("lookup_out")
        gathered = [sem(f"gathered{g}") for g in range(len(GROUPS))]
        turned_rows = sem("turned_rows")
        out_even = sem("out_even")
        out_odd = sem("out_odd")
        placed = sem("placed")
        gram_done = sem("gram_done")
        gram_out_v = sem("gram_out_v")
        gram_out_s = sem("gram_out_s")
        hid1_done = sem("hid1_done")
        hid1_out = sem("hid1_out")
        hid2_done = sem("hid2_done")
        hid2_out = sem("hid2_out")
        y_done = sem("y_done")
        y_out = sem("y_out")
        stored = sem("stored")

        block = ctx.enter_context(nc.Block())

        @block.sync
        def _(sp):
            sp.dma_start(index[:, :, :], ids).then_inc(index_in, 16)

            def load_w1(s):
                sp.dma_start(w1_sb[:, s, :], w1[:, s, :]).then_inc(w1_in[s], 16)

            w1_slots = [SLOTS] + list(range(SLOTS))
            for n in range(LOOKUPS):
                if n >= AHEAD:
                    sp.wait_ge(high_set, n - AHEAD + 1)
                sp.dma_start(ids_i[:, n, :], ids_rows[n:n + 1, :].to_broadcast([P, BATCH])).then_inc(ids_in[n], 16)
                sp.dma_start(table_sb[:, n, :], padded[n, :, :]).then_inc(table_in[n], 16)
                if n >= AHEAD:
                    load_w1(w1_slots.pop(0))
            sp.dma_start(resident[:, 0, :], dense_t).then_inc(dense_in, 16)
            for n in range(AHEAD):
                sp.wait_ge(high_set, LOOKUPS - AHEAD + n + 1)
                load_w1(w1_slots.pop(0))
            sp.dma_start(w3_sb[:, :], w3).then_inc(small_in, 16)
            sp.dma_start(b1_sb[:, :], b1).then_inc(small_in, 16)
            sp.dma_start(b2_sb[:, :], b2).then_inc(small_in, 16)
            for s in w1_slots:
                load_w1(s)
            sp.dma_start(w2_sb[:, :, :], w2).then_inc(w2_in, 16)
            sp.wait_ge(y_out, TILES + 1)
            sp.dma_start(out, y_sb[:, :]).then_inc(stored, 16)
            sp.wait_ge(stored, 16)

        @block.gpsimd
        def _(pool):
            nc.gpsimd.iota(row_id_i[:, :], pattern=[[1, ROW_CHUNKS]], base=0,
                           channel_multiplier=ROW_CHUNKS).then_inc(row_id_set, 1)
            nc.gpsimd.memset(ident[:, :], 0.0).then_inc(ident_set, 1)
            pool.wait_ge(ident_set, 1)
            nc.gpsimd.affine_select(out=ident[:, :], in_=ident[:, :], compare_op=ALU.not_equal, fill=1.0,
                                    base=0, pattern=[[-1, P]], channel_multiplier=1).then_inc(ident_set, 1)
            pool.wait_ge(index_in, 16)
            for t in range(TILES):
                for g, group in enumerate(GROUPS):
                    pool.wait_ge(turned_rows, t * len(GROUPS) + g + 1)
                    for n in group:
                        f = GATHER_TABLES[n]
                        pool.indirect_dma_start(
                            rows[:, n, :], None, tables[f],
                            bass.IndirectOffsetOnAxis(ap=index[:, t, f:f + 1], axis=0),
                        ).then_inc(gathered[g], 16)

        @block.tensor
        def _(pe):
            pe.sem_inc(turned_rows, len(GROUPS))
            pe.sem_inc(gram_done, 1)

            def look_up(n):
                if n >= 2:
                    pe.wait_ge(lookup_out, n - 1)
                for part, part_set in enumerate((high_set, low_set)):
                    pe.wait_ge(part_set, n + 1)
                    for c in range(ROW_CHUNKS):
                        if part == 0 and c < DVE_CHUNKS:
                            pe.wait_ge(onehot_set_v, DVE_CHUNKS * n + c + 1)
                        elif part == 0:
                            pe.wait_ge(onehot_set_s, n + 1)
                        last = nc.tensor.matmul(lookup_ps[n % 2], parts[n % 2][:, part, c * DIM:(c + 1) * DIM],
                                                onehot[n % 2][:, c, :], start=(part == 0 and c == 0),
                                                stop=(part == PARTS - 1 and c == ROW_CHUNKS - 1))
                last.then_inc(lookup_done, 1)

            def turn(t, g):
                group = GROUPS[g]
                pe.wait_ge(gathered[g], t * (16 * len(group)) + 16 * len(group))
                if g % 2 == 0:
                    pe.wait_ge(out_even, t * EVEN + (g // 2 + 1))
                else:
                    pe.wait_ge(out_odd, t * ODD + (g // 2 + 1))
                for n, r in enumerate(group):
                    last = nc.tensor.transpose(turn_ps[g % 2][:, n, :], rows[:, r, :], ident[:, :])
                last.then_inc(turned_rows, 1)

            def gram_round(t, r):
                pe.wait_ge(gram_out_v, t * ROUNDS + (r + 1))
                pe.wait_ge(gram_out_s, t * ROUNDS + (r + 1))
                for n in range(PER_ROUND):
                    b = QUAD * (r * PER_ROUND + n)
                    last = nc.tensor.matmul(gram_ps[r % 2][:, n // PER_BANK, n % PER_BANK, 0:QUAD * COLS],
                                            turned[:, b:b + QUAD, :], turned[:, b:b + QUAD, 1:FEATURES],
                                            start=True, stop=True)
                last.then_inc(gram_done, 1)

            def features_ready(t):
                pe.wait_ge(out_even, t * EVEN + (EVEN + 1))
                pe.wait_ge(out_odd, t * ODD + (ODD + 1))
                pe.wait_ge(placed, t + 1)

            def layer1(t, s):
                if s == SLOTS:
                    k, moving = P, resident[:, 0, bass.ts(t, P)]
                else:
                    k = P if s < SLOTS - 1 else LAST_ROWS
                    moving = pairs[0:k, s, :]
                for c in range(CHUNKS1):
                    last = nc.tensor.matmul(hid1_ps[:, c, :], w1_sb[0:k, s, c * P:(c + 1) * P], moving,
                                            start=(s == SLOTS and c == 0), stop=(s == SLOTS - 1),
                                            skip_group_check=True)
                return last

            def layer2(t):
                for k in range(CHUNKS1):
                    pe.wait_ge(hid1_out, t * CHUNKS1 + (k + 1))
                    for c in range(CHUNKS2):
                        last = nc.tensor.matmul(hid2_ps[:, c, :], w2_sb[:, k, c * P:(c + 1) * P], hid1[:, k, :],
                                                start=(k == 0 and c == 0), stop=(k == CHUNKS1 - 1),
                                                skip_group_check=True)
                last.then_inc(hid2_done, 1)

            def layer3(t):
                for k in range(CHUNKS2):
                    pe.wait_ge(hid2_out, t * CHUNKS2 + (k + 1))
                    last = nc.tensor.matmul(y_ps, w3_sb[:, k:k + 1], hid2[:, k, :],
                                            start=(k == 0), stop=(k == CHUNKS2 - 1))
                last.then_inc(y_done, 1)

            def layers(t, turn_next):
                pe.wait_ge(y_out, t + 1)
                layer1(t, SLOTS)
                if turn_next:
                    turn(t + 1, 0)
                    turn(t + 1, 1)
                pe.wait_ge(gram_out_v, t * ROUNDS + (ROUNDS + 2))
                pe.wait_ge(gram_out_s, t * ROUNDS + (ROUNDS + 2))
                for s in range(SLOTS):
                    last = layer1(t, s)
                last.then_inc(hid1_done, 1)
                if turn_next:
                    turn(t + 1, 2)
                    turn(t + 1, 3)
                layer2(t)

            for n in range(LOOKUPS):
                look_up(n)
                if n == 0:
                    pe.wait_ge(ident_set, 2)
                elif 0 <= n - FIRST_TURN < len(GROUPS):
                    turn(0, n - FIRST_TURN)
            for g in range(LOOKUPS - FIRST_TURN, len(GROUPS)):
                turn(0, g)
            features_ready(0)
            for r in range(ROUNDS):
                gram_round(0, r)
            for s in range(SLOTS + 1):
                pe.wait_ge(w1_in[s], 16)
            pe.wait_ge(w2_in, 16)
            pe.wait_ge(small_in, 48)
            with pe.Fori(0, TILES - 1) as t:
                layers(t, turn_next=True)
                for g in range(4, len(GROUPS)):
                    turn(t + 1, g)
                features_ready(t + 1)
                gram_round(t + 1, 0)
                layer3(t)
                for r in range(1, ROUNDS):
                    gram_round(t + 1, r)
            layers(TILES - 1, turn_next=False)
            layer3(TILES - 1)

        def bring_out_pairs(copy, r, quadrants):
            for q in quadrants:
                blocks = gram_ps[r % 2][LANE * q:LANE * (q + 1), :, :, q * COLS:(q + 1) * COLS]
                for g in range(QUAD):
                    slots = len(range(g, COLS, QUAD))
                    to = pairs[LANE * g:LANE * (g + 1), 0:slots, r * PER_ROUND * QUAD:(r + 1) * PER_ROUND * QUAD]
                    last = copy(
                        to.rearrange("p s (k n q) -> p k n s q", k=2, q=QUAD)[:, :, :, :, q],
                        blocks[:, :, :, g:COLS:QUAD])
            return last

        def bring_out_turned(copy, g):
            group = GROUPS[g]
            return copy(turned[:, :, RESIDENT + group[0]:RESIDENT + group[-1] + 1].rearrange("p b f -> p f b"),
                        turn_ps[g % 2][:, 0:len(group), :])

        @block.vector
        def _(dve):
            dve.sem_inc(out_even, 1)
            dve.sem_inc(gram_out_v, 2)
            nc.vector.memset(turned[:, :, FEATURES:LANE], 0.0).then_inc(pad_set, 1)
            dve.wait_ge(row_id_set, 1)
            nc.vector.tensor_copy(row_id[:, :], row_id_i[:, :]).then_inc(row_id_cast, 1)
            nc.vector.tensor_scalar(minus_row_id[:, :], row_id_i[:, :], -1.0, None, ALU.mult).then_inc(row_id_cast, 1)
            nc.vector.memset(one[:, :], 1.0).then_inc(row_id_cast, 1)
            dve.wait_ge(row_id_cast, 1)

            def turned_out(t, g):
                dve.wait_ge(turned_rows, t * len(GROUPS) + (len(GROUPS) + g + 1))
                bring_out_turned(nc.vector.tensor_copy, g).then_inc(out_even, 1)

            for n in range(LOOKUPS):
                dve.wait_ge(ids_in[n], 16)
                if n >= 2:
                    dve.wait_ge(lookup_done, n - 1)
                for c in range(DVE_CHUNKS):
                    nc.vector.tensor_scalar(onehot[n % 2][:, c, :], ids_i[:, n, :], row_id[:, c:c + 1],
                                            None, ALU.is_equal).then_inc(onehot_set_v, 1)
                dve.wait_ge(high_set, n + 1)
                nc.vector.tensor_tensor(parts[n % 2][:, 1, :], table_sb[:, n, :],
                                        parts[n % 2][:, 0, :].bitcast(fp32), ALU.subtract).then_inc(low_set, 1)
                if 0 <= n - FIRST_TURN - 2 < len(GROUPS) and (n - FIRST_TURN) % 2 == 0:
                    turned_out(0, n - FIRST_TURN - 2)
            for g in range(0, len(GROUPS), 2):
                if g > LOOKUPS - FIRST_TURN - 3:
                    turned_out(0, g)

            def place(t):
                nc.vector.tensor_copy(turned[:, :, 0:RESIDENT].rearrange("p b f -> p f b"),
                                      resident[:, :, bass.ts(t, P)]).then_inc(placed, 1)

            dve.wait_ge(dense_in, 16)
            dve.wait_ge(lookup_out, LOOKUPS)
            place(0)

            def gram_out(t, r):
                dve.wait_ge(gram_done, t * ROUNDS + (r + 2))
                bring_out_pairs(nc.vector.tensor_copy, r, (0, 1)).then_inc(gram_out_v, 1)

            for r in range(ROUNDS):
                gram_out(0, r)
            with dve.Fori(0, TILES - 1) as t:
                place(t + 1)
                for g in range(0, len(GROUPS), 2):
                    turned_out(t + 1, g)
                dve.wait_ge(hid1_done, t + 1)
                for r in range(ROUNDS):
                    gram_out(t + 1, r)

        @block.scalar
        def _(act):
            act.sem_inc(out_odd, 1)
            act.sem_inc(gram_out_s, 2)
            act.sem_inc(y_out, 1)

            def lookup_result(n):
                act.wait_ge(lookup_done, n + 1)
                nc.scalar.copy(resident[:, 1 + n, :], lookup_ps[n % 2]).then_inc(lookup_out, 1)

            def turned_out(t, g):
                act.wait_ge(turned_rows, t * len(GROUPS) + (len(GROUPS) + g + 1))
                bring_out_turned(nc.scalar.copy, g).then_inc(out_odd, 1)

            for n in range(LOOKUPS):
                if n >= 2:
                    lookup_result(n - 2)
                act.wait_ge(ids_in[n], 16)
                if n == 0:
                    act.wait_ge(row_id_cast, 3)
                for c in range(ACT_CHUNKS):
                    last = nc.scalar.activation(distance[n % 2][:, c, :], ids_i[:, n, :], ACT.Square,
                                                bias=minus_row_id[:, DVE_CHUNKS + c:DVE_CHUNKS + c + 1])
                last.then_inc(distance_set, 1)
                act.wait_ge(table_in[n], 16)
                nc.scalar.copy(parts[n % 2][:, 0, :], table_sb[:, n, :]).then_inc(high_set, 1)
                act.wait_ge(distance_set, n + 1)
                nc.scalar.activation(onehot[n % 2][:, DVE_CHUNKS:ROW_CHUNKS, :], distance[n % 2][:, :, :], ACT.Relu,
                                     scale=-1.0, bias=one[:, :]).then_inc(onehot_set_s, 1)
                if 0 <= n - FIRST_TURN - 2 < len(GROUPS) and (n - FIRST_TURN) % 2 == 1:
                    turned_out(0, n - FIRST_TURN - 2)
            lookup_result(LOOKUPS - 2)
            lookup_result(LOOKUPS - 1)
            for g in range(1, len(GROUPS), 2):
                if g > LOOKUPS - FIRST_TURN - 3:
                    turned_out(0, g)
            act.wait_ge(small_in, 48)

            def gram_out(t, r):
                act.wait_ge(gram_done, t * ROUNDS + (r + 2))
                bring_out_pairs(nc.scalar.copy, r, (2, 3)).then_inc(gram_out_s, 1)

            def layers(t, turn_next):
                if turn_next:
                    turned_out(t + 1, 1)
                act.wait_ge(hid1_done, t + 1)
                for c in range(CHUNKS1):
                    nc.scalar.activation(hid1[:, c, :], hid1_ps[:, c, :], ACT.Relu,
                                         bias=b1_sb[:, c:c + 1]).then_inc(hid1_out, 1)
                if turn_next:
                    turned_out(t + 1, 3)
                act.wait_ge(hid2_done, t + 1)
                for c in range(CHUNKS2):
                    nc.scalar.activation(hid2[:, c, :], hid2_ps[:, c, :], ACT.Relu,
                                         bias=b2_sb[:, c:c + 1]).then_inc(hid2_out, 1)

            def result_out(t):
                act.wait_ge(y_done, t + 1)
                nc.scalar.copy(y_sb[:, bass.ts(t, P)], y_ps).then_inc(y_out, 1)

            for r in range(ROUNDS):
                gram_out(0, r)
            with act.Fori(0, TILES - 1) as t:
                layers(t, turn_next=True)
                for g in range(5, len(GROUPS), 2):
                    turned_out(t + 1, g)
                for r in range(ROUNDS):
                    gram_out(t + 1, r)
                    if r == 1:
                        result_out(t)
            layers(TILES - 1, turn_next=False)
            result_out(TILES - 1)


def lay_out_w1(w):
    first, second = np.triu_indices(FEATURES, k=1)
    row_of = {(i, j): n for n, (i, j) in enumerate(zip(first.tolist(), second.tolist()))}
    laid = np.zeros((P, SLOTS + 1, HIDDEN1), w.dtype)
    for j in range(1, FEATURES):
        for i in range(j):
            a, b = sorted((FEATURE_AT[i], FEATURE_AT[j]))
            laid[LANE * ((j - 1) % QUAD) + i, (j - 1) // QUAD] = w[row_of[a, b]]
    laid[:, SLOTS] = w[len(first):]
    return laid


def kernel(**inputs):
    import concourse.bacc as bacc
    from concourse.bass_utils import run_bass_kernel_spmd

    nc = bacc.Bacc("TRN2", target_bir_lowering=False, num_devices=1)
    arrays = {}

    def given(name, array):
        array = np.ascontiguousarray(array)
        arrays[name] = array
        return nc.dram_tensor(name, array.shape, mybir.dt.from_np(array.dtype), kind="ExternalInput").ap()

    x = {name: np.asarray(a) for name, a in inputs.items()}
    laid_tables = np.zeros((LOOKUPS, PADDED_ROWS, DIM), np.float32)
    for n, f in enumerate(MATMUL_TABLES):
        table = x[f"tbl_{f}"]
        laid_tables[n, :table.shape[0]] = table
    dense_t = given("dense_t", x["r_dense_features"].T)
    ids = given("ids", x["ids"].view(np.uint32).reshape(TILES, P, TABLES).transpose(1, 0, 2))
    ids_rows = given("ids_rows", x["ids"].T[MATMUL_TABLES])
    tables = {f: given(f"tbl_{f}", x[f"tbl_{f}"]) for f in GATHER_TABLES}
    padded = given("padded", laid_tables.reshape(LOOKUPS, P, ROW_CHUNKS * DIM))
    w1 = given("w1", lay_out_w1(x["W_top1"]))
    w2 = given("w2", x["W_top2"].reshape(CHUNKS1, P, HIDDEN2).transpose(1, 0, 2))
    w3 = given("w3", x["W_top3"].reshape(CHUNKS2, P).T)
    b1 = given("b1", x["b_top1"].reshape(CHUNKS1, P).T)
    b2 = given("b2", x["b_top2"].reshape(CHUNKS2, P).T)
    out = nc.dram_tensor("y", (1, BATCH), mybir.dt.float32, kind="ExternalOutput").ap()
    dlrm_tower(nc, dense_t, ids, ids_rows, tables, padded, w1, w2, w3, b1, b2, out)
    result = run_bass_kernel_spmd(nc, [arrays], core_ids=[0])
    return result.results[0]["y"].reshape(BATCH, 1)
```

```python
import concourse.bass as bass
import concourse.mybir as mybir
import numpy as np
from contextlib import ExitStack

P = 128
BATCH = 512
DIM = 128
TABLES = 26
FEATURES = TABLES + 1
HIDDEN1, HIDDEN2 = 512, 256
TILES = BATCH // P
CHUNKS1 = HIDDEN1 // P
CHUNKS2 = HIDDEN2 // P

MATMUL_TABLES = [1, 8, 14, 17, 18, 19, 20, 21]
LOOKUPS = len(MATMUL_TABLES)
GATHER_TABLES = [f for f in range(TABLES) if f not in MATMUL_TABLES]
ROW_CHUNKS = 8
PADDED_ROWS = P * ROW_CHUNKS
HALF = ROW_CHUNKS * DIM // 2
DVE_CHUNKS = [6, 6, 6, 7, 6, 7, 6, 7]
DVE_BEFORE = [sum(DVE_CHUNKS[:n]) for n in range(LOOKUPS)]
MAX_ACT_CHUNKS = ROW_CHUNKS - min(DVE_CHUNKS)
AHEAD = 3
PARTS = 2

RESIDENT = 1 + LOOKUPS
FEATURE_AT = [0] + [f + 1 for f in MATMUL_TABLES] + [f + 1 for f in GATHER_TABLES]

GROUP = 4
BEFORE_LAST = len(GATHER_TABLES) - 1
GROUPS = [list(range(a, min(a + GROUP, BEFORE_LAST))) for a in range(0, BEFORE_LAST, GROUP)] + [[BEFORE_LAST]]
EVEN = len(GROUPS[0::2])
ODD = len(GROUPS[1::2])

TURNED_BEHIND = [[], [], [0], [1], [2], [3], [4, 5], []]

WARM_UPS = 8

QUAD = 4
LANE = P // QUAD
NINE = FEATURES // 3
SLOTS = -(-NINE // 2)
UNDER = (0, 2)
OVER = (1, 0)
OVER_BLOCKS = (2, 1)
SHARED = 2
ROUND_QUADS = [8, 12, 12]
ROUNDS = len(ROUND_QUADS)
FIRST_QUAD = [sum(ROUND_QUADS[:r]) for r in range(ROUNDS)]


def dlrm_tower(nc, dense_t, ids, ids_rows, tables, padded, w1, w2, w3, b1, b2, out):
    fp32, fp32r = mybir.dt.float32, mybir.dt.float32r
    i32, u32 = mybir.dt.int32, mybir.dt.uint32
    ALU, ACT = mybir.AluOpType, mybir.ActivationFunctionType

    ctx = ExitStack()
    with ctx:
        def sb(name, shape, dt=fp32):
            return ctx.enter_context(nc.sbuf_tensor(name, shape, dt))

        def ps(name, shape):
            return ctx.enter_context(nc.psum_tensor(name, shape, fp32))

        def sem(name):
            return ctx.enter_context(nc.semaphore(name))

        ident = sb("ident", [P, P])
        index = sb("index", [P, TILES, TABLES], u32)
        rows = sb("rows", [P, len(GATHER_TABLES), DIM])
        resident = sb("resident", [P, RESIDENT, BATCH])
        turned = sb("turned", [P, P, LANE])
        pairs = sb("pairs", [P, SLOTS, P])

        row_id_i = sb("row_id_i", [P, ROW_CHUNKS], i32)
        row_id = sb("row_id", [P, ROW_CHUNKS])
        minus_row_id = sb("minus_row_id", [P, ROW_CHUNKS])
        one = sb("one", [P, 1])
        distance = [sb(f"distance{n}", [P, MAX_ACT_CHUNKS, BATCH]) for n in range(2)]
        ids_i = sb("ids_i", [P, LOOKUPS, BATCH], i32)
        table_sb = sb("table_sb", [P, LOOKUPS, ROW_CHUNKS * DIM])
        parts = [sb(f"parts{n}", [P, PARTS, ROW_CHUNKS * DIM], fp32r) for n in range(2)]
        onehot = [sb(f"onehot{n}", [P, ROW_CHUNKS, BATCH], fp32r) for n in range(2)]

        w1_sb = sb("w1_sb", [P, SLOTS + 1, HIDDEN1])
        w2_sb = sb("w2_sb", [P, CHUNKS1, HIDDEN2])
        w3_sb = sb("w3_sb", [P, CHUNKS2])
        b1_sb = sb("b1_sb", [P, CHUNKS1])
        b2_sb = sb("b2_sb", [P, CHUNKS2])
        hid1 = sb("hid1", [P, CHUNKS1, P])
        hid2 = sb("hid2", [P, CHUNKS2, P])
        y_sb = sb("y_sb", [1, BATCH])

        turn_ps = [ps(f"turn_ps{n}", [P, GROUP, P]) for n in range(2)]
        gram_bank = [ps(f"gram_bank{r}", [P, BATCH]) for r in range(ROUNDS)]
        gram_ps = [gram_bank[r][:, 0:ROUND_QUADS[r] * FEATURES].rearrange("p (n f) -> p n f", f=FEATURES)
                   for r in range(ROUNDS)]
        lookup_ps = [gram_bank[r][:, :] for r in (1, 2)]
        own_hid1_ps = [ps(f"own_hid1_ps{n}", [P, P]) for n in range(2)]
        hid1_ps = [gram_bank[0][:, 0:P], gram_bank[1][:, 0:P], own_hid1_ps[0][:, :], own_hid1_ps[1][:, :]]
        last_ps = ps("last_ps", [P, CHUNKS2 + 1, P])
        hid2_ps = [last_ps[:, c, :] for c in range(CHUNKS2)]
        last_hid2_ps = [turn_ps[c][:, 0, :] for c in range(CHUNKS2)]
        y_ps = last_ps[0:1, CHUNKS2, :]

        ident_set = sem("ident_set")
        row_id_set = sem("row_id_set")
        row_id_cast = sem("row_id_cast")
        pad_set = sem("pad_set")
        index_in = sem("index_in")
        ids_in = [sem(f"ids_in{n}") for n in range(LOOKUPS)]
        table_in = [[sem(f"table_in{h}_{n}") for n in range(LOOKUPS)] for h in range(2)]
        dense_in = sem("dense_in")
        w1_in = [sem(f"w1_in{s}") for s in range(SLOTS + 1)]
        w2_in = sem("w2_in")
        small_in = sem("small_in")
        high_set = sem("high_set")
        low_set = sem("low_set")
        onehot_set_v = sem("onehot_set_v")
        onehot_set_s = sem("onehot_set_s")
        distance_set = sem("distance_set")
        lookup_done = sem("lookup_done")
        lookup_out = sem("lookup_out")
        gathered = [sem(f"gathered{g}") for g in range(len(GROUPS))]
        turned_rows = sem("turned_rows")
        out_even = sem("out_even")
        out_odd = sem("out_odd")
        placed = sem("placed")
        last_placed = sem("last_placed")
        gram_done = sem("gram_done")
        gram_out_v = sem("gram_out_v")
        gram_out_s = sem("gram_out_s")
        under_out_v = sem("under_out_v")
        under_out_s = sem("under_out_s")
        shared_free = sem("shared_free")
        hid1_done = sem("hid1_done")
        hid1_out = sem("hid1_out")
        hid2_done = sem("hid2_done")
        hid2_out = sem("hid2_out")
        y_done = sem("y_done")
        y_out = sem("y_out")
        stored = sem("stored")

        block = ctx.enter_context(nc.Block())

        @block.sync
        def _(sp):
            sp.dma_start(index[:, :, :], ids).then_inc(index_in, 16)

            def load_w1(s):
                sp.dma_start(w1_sb[:, s, :], w1[:, s, :]).then_inc(w1_in[s], 16)

            w1_slots = [SLOTS] + list(range(SLOTS))
            for n in range(LOOKUPS):
                if n >= AHEAD:
                    sp.wait_ge(high_set, 2 * (n - AHEAD + 1))
                sp.dma_start(ids_i[:, n, :], ids_rows[n:n + 1, :].to_broadcast([P, BATCH])).then_inc(ids_in[n], 16)
                for h in range(2):
                    sp.dma_start(table_sb[:, n, h * HALF:(h + 1) * HALF],
                                 padded[n, :, h * HALF:(h + 1) * HALF]).then_inc(table_in[h][n], 16)
                if n >= AHEAD:
                    load_w1(w1_slots.pop(0))
            sp.dma_start(resident[:, 0, :], dense_t).then_inc(dense_in, 16)
            for n, s in enumerate(w1_slots):
                sp.wait_ge(high_set, 2 * (LOOKUPS - AHEAD + n + 1))
                load_w1(s)
            sp.dma_start(w3_sb[:, :], w3).then_inc(small_in, 16)
            sp.dma_start(b1_sb[:, :], b1).then_inc(small_in, 16)
            sp.dma_start(b2_sb[:, :], b2).then_inc(small_in, 16)
            sp.dma_start(w2_sb[:, :, :], w2).then_inc(w2_in, 16)
            sp.wait_ge(y_out, TILES + 1)
            sp.dma_start(out, y_sb[:, :]).then_inc(stored, 16)
            sp.wait_ge(stored, 16)

        @block.gpsimd
        def _(pool):
            nc.gpsimd.iota(row_id_i[:, :], pattern=[[1, ROW_CHUNKS]], base=0,
                           channel_multiplier=ROW_CHUNKS).then_inc(row_id_set, 1)
            nc.gpsimd.memset(ident[:, :], 0.0).then_inc(ident_set, 1)
            pool.wait_ge(ident_set, 1)
            nc.gpsimd.affine_select(out=ident[:, :], in_=ident[:, :], compare_op=ALU.not_equal, fill=1.0,
                                    base=0, pattern=[[-1, P]], channel_multiplier=1).then_inc(ident_set, 1)
            pool.wait_ge(index_in, 16)
            for t in range(TILES):
                for g, group in enumerate(GROUPS):
                    pool.wait_ge(turned_rows, t * len(GROUPS) + g + 1)
                    for n in group:
                        f = GATHER_TABLES[n]
                        pool.indirect_dma_start(
                            rows[:, n, :], None, tables[f],
                            bass.IndirectOffsetOnAxis(ap=index[:, t, f:f + 1], axis=0),
                        ).then_inc(gathered[g], 16)

        @block.tensor
        def _(pe):
            pe.sem_inc(turned_rows, len(GROUPS))

            def look_up(n):
                if n >= 2:
                    pe.wait_ge(lookup_out, n - 1)
                for part in range(PARTS):
                    if part == 1:
                        pe.wait_ge(low_set, n + 1)
                    for c in range(ROW_CHUNKS):
                        if part == 0 and c % (ROW_CHUNKS // 2) == 0:
                            pe.wait_ge(high_set, 2 * n + 1 + c // (ROW_CHUNKS // 2))
                        if part == 0 and c < DVE_CHUNKS[n]:
                            pe.wait_ge(onehot_set_v, DVE_BEFORE[n] + c + 1)
                        elif part == 0:
                            pe.wait_ge(onehot_set_s, n + 1)
                        last = nc.tensor.matmul(lookup_ps[(n + LOOKUPS) % 2], parts[n % 2][:, part, c * DIM:(c + 1) * DIM],
                                                onehot[n % 2][:, c, :], start=(part == 0 and c == 0),
                                                stop=(part == PARTS - 1 and c == ROW_CHUNKS - 1))
                last.then_inc(lookup_done, 1)

            def turn(t, g):
                group = GROUPS[g]
                pe.wait_ge(gathered[g], t * (16 * len(group)) + 16 * len(group))
                if g % 2 == 0:
                    pe.wait_ge(out_even, t * EVEN + (g // 2 + 1))
                else:
                    pe.wait_ge(out_odd, t * ODD + (g // 2 + 1))
                for n, r in enumerate(group):
                    last = nc.tensor.transpose(turn_ps[g % 2][:, n, :], rows[:, r, :], ident[:, :])
                last.then_inc(turned_rows, 1)

            def gram_round(r):
                for n in range(ROUND_QUADS[r]):
                    for q in range(QUAD):
                        b = QUAD * (FIRST_QUAD[r] + n) + q
                        last = nc.tensor.matmul(gram_ps[r][LANE * q:LANE * (q + 1), n, :], turned[:, b, :],
                                                turned[:, b, 0:FEATURES], start=True, stop=True,
                                                tile_position=(0, LANE * q))
                last.then_inc(gram_done, 1)

            def features_ready(t):
                pe.wait_ge(out_even, t * EVEN + (EVEN + 1))
                pe.wait_ge(out_odd, t * ODD + (ODD + 1))
                pe.wait_ge(placed, t + 1)

            def layer1_dense(t, c):
                nc.tensor.matmul(hid1_ps[c], w1_sb[:, SLOTS, c * P:(c + 1) * P], resident[:, 0, bass.ts(t, P)],
                                 start=True, stop=False)

            def layer1_pairs(c):
                for s in range(SLOTS):
                    last = nc.tensor.matmul(hid1_ps[c], w1_sb[:, s, c * P:(c + 1) * P], pairs[:, s, :],
                                            start=False, stop=(s == SLOTS - 1))
                last.then_inc(hid1_done, 1)

            def layer2(t, k):
                pe.wait_ge(hid1_out, t * CHUNKS1 + (k + 1))
                if k == 0:
                    pe.wait_ge(y_out, t + 1)
                for c in range(CHUNKS2):
                    last = nc.tensor.matmul(hid2_ps[c], w2_sb[:, k, c * P:(c + 1) * P], hid1[:, k, :],
                                            start=(k == 0 and c == 0), stop=(k == CHUNKS1 - 1),
                                            skip_group_check=True)
                if k == CHUNKS1 - 1:
                    last.then_inc(hid2_done, CHUNKS2)

            def last_layer2(t, k):
                pe.wait_ge(hid1_out, t * CHUNKS1 + (k + 1))
                for c in range(CHUNKS2):
                    product = nc.tensor.matmul(last_hid2_ps[c], w2_sb[:, k, c * P:(c + 1) * P], hid1[:, k, :],
                                               start=(k == 0), stop=(k == CHUNKS1 - 1))
                    if k == CHUNKS1 - 1:
                        product.then_inc(hid2_done, 1)

            def layer3(t):
                for k in range(CHUNKS2):
                    pe.wait_ge(hid2_out, t * CHUNKS2 + (k + 1))
                    last = nc.tensor.matmul(y_ps, w3_sb[:, k:k + 1], hid2[:, k, :],
                                            start=(k == 0), stop=(k == CHUNKS2 - 1))
                last.then_inc(y_done, 1)

            def layer1_start(t):
                layer1_dense(t, 2)
                layer1_dense(t, 3)
                for c in range(2):
                    pe.wait_ge(gram_out_v, t * ROUNDS + (c + 1))
                    pe.wait_ge(gram_out_s, t * ROUNDS + (c + 1))
                    layer1_dense(t, c)
                pe.wait_ge(gram_out_v, t * ROUNDS + ROUNDS)
                pe.wait_ge(gram_out_s, t * ROUNDS + ROUNDS)

            pe.wait_ge(pad_set, 2)
            for _ in range(WARM_UPS):
                nc.tensor.matmul(hid1_ps[2], pairs[:, 0, :], pairs[:, 0, :], start=True, stop=True)

            for n in range(LOOKUPS):
                look_up(n)
                if n == 0:
                    pe.wait_ge(ident_set, 2)
                for g in TURNED_BEHIND[n]:
                    turn(0, g)
            pe.wait_ge(last_placed, 1)
            features_ready(0)
            gram_round(0)
            gram_round(1)
            pe.wait_ge(lookup_out, LOOKUPS)
            gram_round(2)
            for s in range(SLOTS + 1):
                pe.wait_ge(w1_in[s], 16)
            pe.wait_ge(w2_in, 16)
            pe.wait_ge(small_in, 48)
            with pe.Fori(0, TILES - 1) as t:
                turn(t + 1, 0)
                turn(t + 1, 1)
                layer1_start(t)
                layer1_pairs(0)
                turn(t + 1, 2)
                layer1_pairs(1)
                layer2(t, 0)
                layer1_pairs(2)
                turn(t + 1, 3)
                layer2(t, 1)
                layer1_pairs(3)
                turn(t + 1, 4)
                turn(t + 1, 5)
                layer2(t, 2)
                layer2(t, 3)
                features_ready(t + 1)
                gram_round(0)
                pe.wait_ge(hid2_out, t * CHUNKS2 + CHUNKS2)
                layer3(t)
                gram_round(1)
                gram_round(2)
            layer1_start(TILES - 1)
            layer1_pairs(0)
            layer1_pairs(1)
            pe.wait_ge(y_out, TILES)
            pe.wait_ge(out_even, TILES * EVEN + 1)
            pe.wait_ge(out_odd, TILES * ODD + 1)
            last_layer2(TILES - 1, 0)
            layer1_pairs(2)
            last_layer2(TILES - 1, 1)
            layer1_pairs(3)
            last_layer2(TILES - 1, 2)
            last_layer2(TILES - 1, 3)
            layer3(TILES - 1)

        def bring_out_columns(copy, r, q, g, lanes, block):
            first = NINE * block + g % 2
            slots = len(range(g % 2, NINE, 2))
            to = pairs[LANE * g:LANE * g + lanes, 0:slots,
                       QUAD * FIRST_QUAD[r]:QUAD * (FIRST_QUAD[r] + ROUND_QUADS[r])]
            return copy(to.rearrange("p s (n q) -> p n s q", q=QUAD)[:, :, :, q],
                        gram_ps[r][LANE * q:LANE * q + lanes, :, first:NINE * (block + 1):2])

        def bring_out_under(copy, r, q):
            for g in range(QUAD):
                last = bring_out_columns(copy, r, q, g, LANE, UNDER[g // 2])
            return last

        def bring_out_over(copy, r, q, quadrants):
            for g in quadrants:
                last = bring_out_columns(copy, r, q, g, NINE * OVER_BLOCKS[g // 2], OVER[g // 2])
            return last

        def bring_out_turned(copy, g):
            group = GROUPS[g]
            return copy(turned[:, :, RESIDENT + group[0]:RESIDENT + group[-1] + 1].rearrange("p b f -> p f b"),
                        turn_ps[g % 2][:, 0:len(group), :])

        @block.vector
        def _(dve):
            dve.sem_inc(out_even, 1)
            nc.vector.memset(pairs[:, :, :], 0.0).then_inc(pad_set, 1)
            nc.vector.memset(turned[:, :, FEATURES:LANE], 0.0).then_inc(pad_set, 1)
            dve.wait_ge(row_id_set, 1)
            nc.vector.tensor_copy(row_id[:, :], row_id_i[:, :]).then_inc(row_id_cast, 1)
            nc.vector.tensor_scalar(minus_row_id[:, :], row_id_i[:, :], -1.0, None, ALU.mult).then_inc(row_id_cast, 1)
            nc.vector.memset(one[:, :], 1.0).then_inc(row_id_cast, 1)
            dve.wait_ge(row_id_cast, 1)

            def turned_out(t, g):
                dve.wait_ge(turned_rows, t * len(GROUPS) + (len(GROUPS) + g + 1))
                bring_out_turned(nc.vector.tensor_copy, g).then_inc(out_even, 1)

            for n in range(LOOKUPS):
                dve.wait_ge(ids_in[n], 16)
                if n >= 2:
                    dve.wait_ge(lookup_done, n - 1)
                for c in range(DVE_CHUNKS[n]):
                    nc.vector.tensor_scalar(onehot[n % 2][:, c, :], ids_i[:, n, :], row_id[:, c:c + 1],
                                            None, ALU.is_equal).then_inc(onehot_set_v, 1)
                dve.wait_ge(high_set, 2 * n + 2)
                nc.vector.tensor_tensor(parts[n % 2][:, 1, :], table_sb[:, n, :],
                                        parts[n % 2][:, 0, :].bitcast(fp32), ALU.subtract).then_inc(low_set, 1)
                for g in TURNED_BEHIND[n - 2] if n >= 2 else []:
                    if g % 2 == 0:
                        turned_out(0, g)
            def place(t, known=RESIDENT):
                nc.vector.tensor_copy(turned[:, :, 0:known].rearrange("p b f -> p f b"),
                                      resident[:, 0:known, bass.ts(t, P)]).then_inc(placed, 1)

            dve.wait_ge(pad_set, 2)
            dve.wait_ge(dense_in, 16)
            dve.wait_ge(lookup_out, LOOKUPS - 1)
            place(0, RESIDENT - 1)
            for g in TURNED_BEHIND[LOOKUPS - 2]:
                if g % 2 == 0:
                    turned_out(0, g)
            def gram_out(t, r):
                dve.wait_ge(gram_done, t * ROUNDS + (r + 1))
                bring_out_under(nc.vector.tensor_copy, r, 1).then_inc(under_out_v, 1)
                bring_out_under(nc.vector.tensor_copy, r, 0).then_inc(under_out_v, 1)
                dve.wait_ge(under_out_v, 2 * t * ROUNDS + (2 * r + 1))
                bring_out_over(nc.vector.tensor_copy, r, 1, range(0, SHARED)).then_inc(shared_free, 1)
                dve.wait_ge(under_out_v, 2 * t * ROUNDS + (2 * r + 2))
                bring_out_over(nc.vector.tensor_copy, r, 0, range(QUAD)).then_inc(gram_out_v, 1)

            for r in range(ROUNDS):
                gram_out(0, r)
            with dve.Fori(0, TILES - 1) as t:
                dve.wait_ge(lookup_out, LOOKUPS)
                place(t + 1)
                for g in range(0, len(GROUPS), 2):
                    turned_out(t + 1, g)
                dve.wait_ge(hid1_done, t * CHUNKS1 + CHUNKS1)
                for r in range(ROUNDS):
                    gram_out(t + 1, r)

        @block.scalar
        def _(act):
            act.sem_inc(out_odd, 1)
            act.sem_inc(y_out, 1)

            def lookup_result(n):
                act.wait_ge(lookup_done, n + 1)
                if n == LOOKUPS - 1:
                    nc.scalar.copy(turned[:, :, LOOKUPS], lookup_ps[(n + LOOKUPS) % 2][:, 0:P]).then_inc(last_placed, 1)
                nc.scalar.copy(resident[:, 1 + n, :], lookup_ps[(n + LOOKUPS) % 2]).then_inc(lookup_out, 1)

            def turned_out(t, g):
                act.wait_ge(turned_rows, t * len(GROUPS) + (len(GROUPS) + g + 1))
                bring_out_turned(nc.scalar.copy, g).then_inc(out_odd, 1)

            def squares(n):
                act.wait_ge(ids_in[n], 16)
                if n == 0:
                    act.wait_ge(row_id_cast, 3)
                for c in range(DVE_CHUNKS[n], ROW_CHUNKS):
                    last = nc.scalar.activation(distance[n % 2][:, c - DVE_CHUNKS[n], :], ids_i[:, n, :], ACT.Square,
                                                bias=minus_row_id[:, c:c + 1])
                last.then_inc(distance_set, 1)

            for n in range(LOOKUPS):
                if n >= 2:
                    lookup_result(n - 2)
                    for g in TURNED_BEHIND[n - 2]:
                        if g % 2 == 1:
                            turned_out(0, g)
                if n == 0:
                    squares(n)
                for h in range(2):
                    act.wait_ge(table_in[h][n], 16)
                    nc.scalar.copy(parts[n % 2][:, 0, h * HALF:(h + 1) * HALF],
                                   table_sb[:, n, h * HALF:(h + 1) * HALF]).then_inc(high_set, 1)
                if n > 0:
                    squares(n)
                act.wait_ge(distance_set, n + 1)
                nc.scalar.activation(onehot[n % 2][:, DVE_CHUNKS[n]:ROW_CHUNKS, :],
                                     distance[n % 2][:, 0:ROW_CHUNKS - DVE_CHUNKS[n], :], ACT.Relu,
                                     scale=-1.0, bias=one[:, :]).then_inc(onehot_set_s, 1)
            lookup_result(LOOKUPS - 2)
            for g in TURNED_BEHIND[LOOKUPS - 2]:
                if g % 2 == 1:
                    turned_out(0, g)
            lookup_result(LOOKUPS - 1)
            act.wait_ge(small_in, 48)
            act.wait_ge(pad_set, 2)

            def gram_out(t, r):
                act.wait_ge(gram_done, t * ROUNDS + (r + 1))
                bring_out_under(nc.scalar.copy, r, 2).then_inc(under_out_s, 1)
                bring_out_under(nc.scalar.copy, r, 3).then_inc(under_out_s, 1)
                act.wait_ge(under_out_s, 2 * t * ROUNDS + (2 * r + 1))
                bring_out_over(nc.scalar.copy, r, 2, range(QUAD))
                act.wait_ge(under_out_s, 2 * t * ROUNDS + (2 * r + 2))
                bring_out_over(nc.scalar.copy, r, 3, range(QUAD))
                act.wait_ge(shared_free, t * ROUNDS + (r + 1))
                bring_out_over(nc.scalar.copy, r, 1, range(SHARED, QUAD)).then_inc(gram_out_s, 1)

            def hid1_relu(t, c):
                act.wait_ge(hid1_done, t * CHUNKS1 + (c + 1))
                nc.scalar.activation(hid1[:, c, :], hid1_ps[c], ACT.Relu, bias=b1_sb[:, c:c + 1]).then_inc(hid1_out, 1)

            def hid2_relu(t, c, source):
                act.wait_ge(hid2_done, t * CHUNKS2 + (c + 1))
                nc.scalar.activation(hid2[:, c, :], source[c], ACT.Relu, bias=b2_sb[:, c:c + 1]).then_inc(hid2_out, 1)

            def result_out(t):
                act.wait_ge(y_done, t + 1)
                nc.scalar.copy(y_sb[:, bass.ts(t, P)], y_ps).then_inc(y_out, 1)

            for r in range(ROUNDS):
                gram_out(0, r)
            with act.Fori(0, TILES - 1) as t:
                turned_out(t + 1, 1)
                for c in range(CHUNKS1 - 1):
                    hid1_relu(t, c)
                turned_out(t + 1, 3)
                hid1_relu(t, CHUNKS1 - 1)
                turned_out(t + 1, 5)
                for c in range(CHUNKS2):
                    hid2_relu(t, c, hid2_ps)
                gram_out(t + 1, 0)
                result_out(t)
                for r in range(1, ROUNDS):
                    gram_out(t + 1, r)
            for c in range(CHUNKS1):
                hid1_relu(TILES - 1, c)
            for c in range(CHUNKS2):
                hid2_relu(TILES - 1, c, last_hid2_ps)
            result_out(TILES - 1)


def column_of(g, s, i):
    n = 2 * s + g % 2
    block = OVER[g // 2] if i < NINE * OVER_BLOCKS[g // 2] else UNDER[g // 2]
    return NINE * block + n if n < NINE else None


def lay_out_w1(w):
    first, second = np.triu_indices(FEATURES, k=1)
    row_of = {(i, j): n for n, (i, j) in enumerate(zip(first.tolist(), second.tolist()))}
    laid = np.zeros((P, SLOTS + 1, HIDDEN1), w.dtype)
    for g in range(QUAD):
        for s in range(SLOTS):
            for i in range(FEATURES):
                j = column_of(g, s, i)
                if j is not None and j != i:
                    row = row_of.pop(tuple(sorted((FEATURE_AT[i], FEATURE_AT[j]))), None)
                    if row is not None:
                        laid[LANE * g + i, s] = w[row]
    assert not row_of
    laid[:, SLOTS] = w[len(first):]
    return laid


def kernel(**inputs):
    import concourse.bacc as bacc
    from concourse.bass_utils import run_bass_kernel_spmd

    nc = bacc.Bacc("TRN2", target_bir_lowering=False, num_devices=1)
    arrays = {}

    def given(name, array):
        array = np.ascontiguousarray(array)
        arrays[name] = array
        return nc.dram_tensor(name, array.shape, mybir.dt.from_np(array.dtype), kind="ExternalInput").ap()

    x = {name: np.asarray(a) for name, a in inputs.items()}
    laid_tables = np.zeros((LOOKUPS, PADDED_ROWS, DIM), np.float32)
    for n, f in enumerate(MATMUL_TABLES):
        table = x[f"tbl_{f}"]
        laid_tables[n, :table.shape[0]] = table
    dense_t = given("dense_t", x["r_dense_features"].T)
    ids = given("ids", x["ids"].view(np.uint32).reshape(TILES, P, TABLES).transpose(1, 0, 2))
    ids_rows = given("ids_rows", x["ids"].T[MATMUL_TABLES])
    tables = {f: given(f"tbl_{f}", x[f"tbl_{f}"]) for f in GATHER_TABLES}
    padded = given("padded", laid_tables.reshape(LOOKUPS, P, ROW_CHUNKS * DIM))
    w1 = given("w1", lay_out_w1(x["W_top1"]))
    w2 = given("w2", x["W_top2"].reshape(CHUNKS1, P, HIDDEN2).transpose(1, 0, 2))
    w3 = given("w3", x["W_top3"].reshape(CHUNKS2, P).T)
    b1 = given("b1", x["b_top1"].reshape(CHUNKS1, P).T)
    b2 = given("b2", x["b_top2"].reshape(CHUNKS2, P).T)
    out = nc.dram_tensor("y", (1, BATCH), mybir.dt.float32, kind="ExternalOutput").ap()
    dlrm_tower(nc, dense_t, ids, ids_rows, tables, padded, w1, w2, w3, b1, b2, out)
    result = run_bass_kernel_spmd(nc, [arrays], core_ids=[0])
    return result.results[0]["y"].reshape(BATCH, 1)
```
